# Optimizing a Trainium2 kernel written in Bass

```python
import numpy as np
import jax
import jax.numpy as jnp

def _softmax(x, axis=-1):
    return jax.nn.softmax(x, axis=axis)

def _gelu(x):
    return jax.nn.gelu(x, approximate=True)

def _silu(x):
    return jax.nn.silu(x)

def _sigmoid(x):
    return jax.nn.sigmoid(x)

def _layernorm(x, axis=-1, eps=1e-05):
    m = jnp.mean(x, axis=axis, keepdims=True)
    v = jnp.var(x, axis=axis, keepdims=True)
    return (x - m) / jnp.sqrt(v + eps)

def _scatter_add(tgt, idx, src, axis=0):
    return tgt.at[idx].add(src)

def _segment_sum(src, seg, n):
    return jax.ops.segment_sum(src, seg, n)
kernel_name = 'mk_pixart_seq_d4_seqx_r8_b6b702'

def setup_inputs(seed: int=0):
    np.random.seed(seed)
    _w = jnp.asarray

    def _rec_inputs():
        import jax
        import jax.numpy as jnp
        _rk = jax.random.key(seed)
        x = -0.0002928 + 1 * jax.random.normal(jax.random.fold_in(_rk, 1), (4, 256, 128), jnp.float32)
        _lenS = 256 - jax.random.randint(jax.random.fold_in(_rk, 7), (4,), 0, max(1, 256 // 4) + 1, jnp.int32)
        _lenS2 = 256 - jax.random.randint(jax.random.fold_in(_rk, 8), (4,), 0, max(1, 256 // 4) + 1, jnp.int32)
        cond_1024 = 0.0061147 + 1.02565 * jax.random.normal(jax.random.fold_in(_rk, 11), (4, 128), jnp.float32)
        _ctx_1024P = jax.random.normal(jax.random.fold_in(_rk, 12), (4, 16, 128), jnp.float32)
        _ctx_1024c = jax.random.dirichlet(jax.random.fold_in(_rk, 512), 0.3 * jnp.ones((16,), jnp.float32), (4, 256))
        _ctx_1024t = jnp.einsum('bsk,bkd->bsd', _ctx_1024c, _ctx_1024P)
        _ctx_1024t = _ctx_1024t * jax.lax.rsqrt(jnp.mean(jnp.square(_ctx_1024t)) + 1e-12) * 0.953939
        ctx_1024 = -0.00265004 + 0.998804 * (_ctx_1024t + 0.3 * jax.random.normal(jax.random.fold_in(_rk, 612), (4, 256, 128), jnp.float32))
        return (x, cond_1024, ctx_1024)
    x, cond_1024, ctx_1024 = _rec_inputs()

    def _L0_xcond_setup():
        import jax, jax.numpy as jnp
        import numpy as np
        LN_EPS = 1e-06

        def _ln(x):
            mu = jnp.mean(x, axis=-1, keepdims=True)
            var = jnp.var(x, axis=-1, keepdims=True)
            return (x - mu) * jax.lax.rsqrt(var + LN_EPS)
        key = jax.random.key(seed)
        H, NH = (128, 16)
        B, N, S = (4, 128, 77)
        MLP = int(H * 4.0)
        ks = jax.random.split(key, 20)
        s = 1.0 / np.sqrt(H)
        return {'x': jax.random.normal(ks[0], (B, N, H), jnp.float32), 'c': jax.random.normal(ks[1], (B, H), jnp.float32), 'context': jax.random.normal(ks[2], (B, S, H), jnp.float32), 'W_mod': jax.random.normal(ks[3], (H, 6 * H), jnp.float32) * s, 'b_mod': jnp.zeros((6 * H,), jnp.float32), 'W_qkv': jax.random.normal(ks[4], (H, 3 * H), jnp.float32) * s, 'b_qkv': jnp.zeros((3 * H,), jnp.float32), 'W_proj': jax.random.normal(ks[5], (H, H), jnp.float32) * s, 'b_proj': jnp.zeros((H,), jnp.float32), 'W_qc': jax.random.normal(ks[6], (H, H), jnp.float32) * s, 'b_qc': jnp.zeros((H,), jnp.float32), 'W_kvc': jax.random.normal(ks[7], (H, 2 * H), jnp.float32) * s, 'b_kvc': jnp.zeros((2 * H,), jnp.float32), 'W_cproj': jax.random.normal(ks[8], (H, H), jnp.float32) * s, 'b_cproj': jnp.zeros((H,), jnp.float32), 'W_mlp1': jax.random.normal(ks[9], (H, MLP), jnp.float32) * s, 'b_mlp1': jnp.zeros((MLP,), jnp.float32), 'W_mlp2': jax.random.normal(ks[10], (MLP, H), jnp.float32) * (1.0 / np.sqrt(MLP)), 'b_mlp2': jnp.zeros((H,), jnp.float32)}
    _L0_xcond_all = _L0_xcond_setup()
    _L0_xcond_in = {k: v for k, v in _L0_xcond_all.items() if k in ('W_mod', 'b_mod', 'W_qkv', 'b_qkv', 'W_proj', 'b_proj', 'W_qc', 'b_qc', 'W_kvc', 'b_kvc', 'W_cproj', 'b_cproj', 'W_mlp1', 'b_mlp1', 'W_mlp2', 'b_mlp2')}
    del _L0_xcond_all

    def _L1_xcond_setup():
        import jax, jax.numpy as jnp
        import numpy as np
        D = 128
        H = 16
        HD = D // H
        MLP = 4 * D
        EPS = 1e-06
        SCALE = HD ** (-0.5)

        def _p(key, shape, s=0.02):
            return jax.random.normal(key, shape, dtype=jnp.float32) * s

        def _ln(x):
            mu = jnp.mean(x, axis=-1, keepdims=True)
            var = jnp.var(x, axis=-1, keepdims=True)
            return (x - mu) * jax.lax.rsqrt(var + EPS)

        def _heads(t):
            B, L, _ = t.shape
            return t.reshape(B, L, H, HD).transpose(0, 2, 1, 3)

        def _attend(q, k, v):
            attn = jnp.einsum('bhnd,bhsd->bhns', q, k) * SCALE
            attn = jax.nn.softmax(attn, axis=-1)
            o = jnp.einsum('bhns,bhsd->bhnd', attn, v)
            B, _, N, _ = q.shape
            return o.transpose(0, 2, 1, 3).reshape(B, N, D)
        key = jax.random.key(seed)
        ks = jax.random.split(key, 24)
        B, N, S = (4, 128, 77)
        return {'x': jax.random.normal(ks[0], (B, N, D), dtype=jnp.float32), 't_emb': jax.random.normal(ks[1], (B, D), dtype=jnp.float32), 'context': jax.random.normal(ks[2], (B, S, D), dtype=jnp.float32), 'adaln_w': _p(ks[3], (D, 6 * D)), 'adaln_b': _p(ks[4], (6 * D,)), 'qkv_w': _p(ks[5], (D, 3 * D)), 'qkv_b': _p(ks[6], (3 * D,)), 'sa_proj_w': _p(ks[7], (D, D)), 'sa_proj_b': _p(ks[8], (D,)), 'q_w': _p(ks[9], (D, D)), 'q_b': _p(ks[10], (D,)), 'kv_w': _p(ks[11], (D, 2 * D)), 'kv_b': _p(ks[12], (2 * D,)), 'ca_proj_w': _p(ks[13], (D, D)), 'ca_proj_b': _p(ks[14], (D,)), 'fc1_w': _p(ks[15], (D, MLP)), 'fc1_b': _p(ks[16], (MLP,)), 'fc2_w': _p(ks[17], (MLP, D)), 'fc2_b': _p(ks[18], (D,))}
    _L1_xcond_all = _L1_xcond_setup()
    _L1_xcond_in = {k: v for k, v in _L1_xcond_all.items() if k in ('adaln_w', 'adaln_b', 'qkv_w', 'qkv_b', 'sa_proj_w', 'sa_proj_b', 'q_w', 'q_b', 'kv_w', 'kv_b', 'ca_proj_w', 'ca_proj_b', 'fc1_w', 'fc1_b', 'fc2_w', 'fc2_b')}
    del _L1_xcond_all

    def _L2_xcond_setup():
        import jax, jax.numpy as jnp
        import numpy as np
        EPS = 1e-05

        def _ada_ln(x, c, W_ss, b_ss):
            mu = jnp.mean(x, axis=-1, keepdims=True)
            var = jnp.mean((x - mu) ** 2, axis=-1, keepdims=True)
            h = (x - mu) / jnp.sqrt(var + EPS)
            ss = jax.nn.silu(c) @ W_ss + b_ss
            scale, bias = jnp.split(ss, 2, axis=-1)
            return (1.0 + scale)[:, None, :] * h + bias[:, None, :]
        key = jax.random.key(seed)
        ks = jax.random.split(key, 12)
        B, Lq, Lkv, H = (8, 256, 64, 128)
        s = 0.02
        return {'x_q': jax.random.normal(ks[0], (B, Lq, H), jnp.float32), 'x_kv': jax.random.normal(ks[1], (B, Lkv, H), jnp.float32), 't_vec': jax.random.normal(ks[2], (B, H), jnp.float32), 'Wq': jax.random.normal(ks[3], (H, H), jnp.float32) * s, 'bq': jnp.zeros((H,), jnp.float32), 'Wkv': jax.random.normal(ks[4], (H, 2 * H), jnp.float32) * s, 'bkv': jnp.zeros((2 * H,), jnp.float32), 'Wp': jax.random.normal(ks[5], (H, H), jnp.float32) * s, 'bp': jnp.zeros((H,), jnp.float32), 'Wss_q': jax.random.normal(ks[6], (H, 2 * H), jnp.float32) * s, 'bss_q': jnp.zeros((2 * H,), jnp.float32), 'Wss_kv': jax.random.normal(ks[7], (H, 2 * H), jnp.float32) * s, 'bss_kv': jnp.zeros((2 * H,), jnp.float32)}
    _L2_xcond_all = _L2_xcond_setup()
    _L2_xcond_in = {k: v for k, v in _L2_xcond_all.items() if k in ('Wq', 'bq', 'Wkv', 'bkv', 'Wp', 'bp', 'Wss_q', 'bss_q', 'Wss_kv', 'bss_kv')}
    del _L2_xcond_all

    def _L3_xcond_setup():
        import jax, jax.numpy as jnp
        import numpy as np
        C = 128
        H = 16
        D = C // H
        WIN = 64
        SHIFT = 32
        TOPK = 16
        HID = 512
        EPS = 1e-06

        def _ln(x):
            x32 = x.astype(jnp.float32)
            m = x32.mean(-1, keepdims=True)
            v = jnp.mean((x32 - m) ** 2, axis=-1, keepdims=True)
            return ((x32 - m) * jax.lax.rsqrt(v + EPS)).astype(x.dtype)

        def _self_attn(h, w_qkv, b_qkv, w_so, b_so):
            B, L, _ = h.shape
            qkv = h @ w_qkv + b_qkv
            qkv = jnp.roll(qkv, -SHIFT, axis=1)
            nw = L // WIN
            qkv = qkv.reshape(B, nw, WIN, 3, H, D)
            q, k, v = (qkv[:, :, :, 0], qkv[:, :, :, 1], qkv[:, :, :, 2])
            scores = jnp.einsum('bnqhd,bnkhd->bnhqk', q, k) / jnp.sqrt(jnp.float32(D)).astype(h.dtype)
            attn = jax.nn.softmax(scores, axis=-1)
            o = jnp.einsum('bnhqk,bnkhd->bnqhd', attn, v).reshape(B, L, C)
            o = jnp.roll(o, SHIFT, axis=1)
            return o @ w_so + b_so

        def _topk_cross_attn(h, ctx, w_q, b_q, w_kv, b_kv, w_co, b_co):
            B, L, _ = h.shape
            Lc = ctx.shape[1]
            q = (h @ w_q + b_q).reshape(B, L, H, D)
            kv = (ctx @ w_kv + b_kv).reshape(B, Lc, 2, H, D)
            k, v = (kv[:, :, 0], kv[:, :, 1])
            scores = jnp.einsum('bqhd,bkhd->bhqk', q, k) / jnp.sqrt(jnp.float32(D)).astype(h.dtype)
            top_s, top_i = jax.lax.top_k(scores, TOPK)
            attn = jax.nn.softmax(top_s, axis=-1)
            v_bh = jnp.transpose(v, (0, 2, 1, 3))
            vg = jnp.take_along_axis(v_bh[:, :, None, :, :], top_i[..., None], axis=3)
            o = jnp.einsum('bhqk,bhqkd->bqhd', attn, vg).reshape(B, L, C)
            return o @ w_co + b_co

        def _swiglu(h, w_m1, b_m1, w_m2, b_m2):
            u = h @ w_m1 + b_m1
            a, b = (u[..., :HID], u[..., HID:])
            return jax.nn.silu(a) * b @ w_m2 + b_m2
        key = jax.random.key(seed)
        ks = jax.random.split(key, 24)
        s = 0.02
        inp = {'x': jax.random.normal(ks[0], (2, 512, C), jnp.float32), 'mod': jax.random.normal(ks[1], (2, C), jnp.float32), 'context': jax.random.normal(ks[2], (2, 128, C), jnp.float32), 'w_ada': jax.random.normal(ks[3], (C, 9 * C), jnp.float32) * s, 'b_ada': jnp.zeros((9 * C,), jnp.float32), 'w_qkv': jax.random.normal(ks[4], (C, 3 * C), jnp.float32) * s, 'b_qkv': jnp.zeros((3 * C,), jnp.float32), 'w_so': jax.random.normal(ks[5], (C, C), jnp.float32) * s, 'b_so': jnp.zeros((C,), jnp.float32), 'w_q': jax.random.normal(ks[6], (C, C), jnp.float32) * s, 'b_q': jnp.zeros((C,), jnp.float32), 'w_kv': jax.random.normal(ks[7], (C, 2 * C), jnp.float32) * s, 'b_kv': jnp.zeros((2 * C,), jnp.float32), 'w_co': jax.random.normal(ks[8], (C, C), jnp.float32) * s, 'b_co': jnp.zeros((C,), jnp.float32), 'w_m1': jax.random.normal(ks[9], (C, 2 * HID), jnp.float32) * s, 'b_m1': jnp.zeros((2 * HID,), jnp.float32), 'w_m2': jax.random.normal(ks[10], (HID, C), jnp.float32) * s, 'b_m2': jnp.zeros((C,), jnp.float32)}
        return inp
    _L3_xcond_all = _L3_xcond_setup()
    _L3_xcond_in = {k: v for k, v in _L3_xcond_all.items() if k in ('w_ada', 'b_ada', 'w_qkv', 'b_qkv', 'w_so', 'b_so', 'w_q', 'b_q', 'w_kv', 'b_kv', 'w_co', 'b_co', 'w_m1', 'b_m1', 'w_m2', 'b_m2')}
    del _L3_xcond_all
    return {'x': x, 'cond_1024': cond_1024, 'ctx_1024': ctx_1024, 'L0_xcond_W_mod': _L0_xcond_in['W_mod'], 'L0_xcond_b_mod': _L0_xcond_in['b_mod'], 'L0_xcond_W_qkv': _L0_xcond_in['W_qkv'], 'L0_xcond_b_qkv': _L0_xcond_in['b_qkv'], 'L0_xcond_W_proj': _L0_xcond_in['W_proj'], 'L0_xcond_b_proj': _L0_xcond_in['b_proj'], 'L0_xcond_W_qc': _L0_xcond_in['W_qc'], 'L0_xcond_b_qc': _L0_xcond_in['b_qc'], 'L0_xcond_W_kvc': _L0_xcond_in['W_kvc'], 'L0_xcond_b_kvc': _L0_xcond_in['b_kvc'], 'L0_xcond_W_cproj': _L0_xcond_in['W_cproj'], 'L0_xcond_b_cproj': _L0_xcond_in['b_cproj'], 'L0_xcond_W_mlp1': _L0_xcond_in['W_mlp1'], 'L0_xcond_b_mlp1': _L0_xcond_in['b_mlp1'], 'L0_xcond_W_mlp2': _L0_xcond_in['W_mlp2'], 'L0_xcond_b_mlp2': _L0_xcond_in['b_mlp2'], 'L1_xcond_adaln_w': _L1_xcond_in['adaln_w'], 'L1_xcond_adaln_b': _L1_xcond_in['adaln_b'], 'L1_xcond_qkv_w': _L1_xcond_in['qkv_w'], 'L1_xcond_qkv_b': _L1_xcond_in['qkv_b'], 'L1_xcond_sa_proj_w': _L1_xcond_in['sa_proj_w'], 'L1_xcond_sa_proj_b': _L1_xcond_in['sa_proj_b'], 'L1_xcond_q_w': _L1_xcond_in['q_w'], 'L1_xcond_q_b': _L1_xcond_in['q_b'], 'L1_xcond_kv_w': _L1_xcond_in['kv_w'], 'L1_xcond_kv_b': _L1_xcond_in['kv_b'], 'L1_xcond_ca_proj_w': _L1_xcond_in['ca_proj_w'], 'L1_xcond_ca_proj_b': _L1_xcond_in['ca_proj_b'], 'L1_xcond_fc1_w': _L1_xcond_in['fc1_w'], 'L1_xcond_fc1_b': _L1_xcond_in['fc1_b'], 'L1_xcond_fc2_w': _L1_xcond_in['fc2_w'], 'L1_xcond_fc2_b': _L1_xcond_in['fc2_b'], 'L2_xcond_Wq': _L2_xcond_in['Wq'], 'L2_xcond_bq': _L2_xcond_in['bq'], 'L2_xcond_Wkv': _L2_xcond_in['Wkv'], 'L2_xcond_bkv': _L2_xcond_in['bkv'], 'L2_xcond_Wp': _L2_xcond_in['Wp'], 'L2_xcond_bp': _L2_xcond_in['bp'], 'L2_xcond_Wss_q': _L2_xcond_in['Wss_q'], 'L2_xcond_bss_q': _L2_xcond_in['bss_q'], 'L2_xcond_Wss_kv': _L2_xcond_in['Wss_kv'], 'L2_xcond_bss_kv': _L2_xcond_in['bss_kv'], 'L3_xcond_w_ada': _L3_xcond_in['w_ada'], 'L3_xcond_b_ada': _L3_xcond_in['b_ada'], 'L3_xcond_w_qkv': _L3_xcond_in['w_qkv'], 'L3_xcond_b_qkv': _L3_xcond_in['b_qkv'], 'L3_xcond_w_so': _L3_xcond_in['w_so'], 'L3_xcond_b_so': _L3_xcond_in['b_so'], 'L3_xcond_w_q': _L3_xcond_in['w_q'], 'L3_xcond_b_q': _L3_xcond_in['b_q'], 'L3_xcond_w_kv': _L3_xcond_in['w_kv'], 'L3_xcond_b_kv': _L3_xcond_in['b_kv'], 'L3_xcond_w_co': _L3_xcond_in['w_co'], 'L3_xcond_b_co': _L3_xcond_in['b_co'], 'L3_xcond_w_m1': _L3_xcond_in['w_m1'], 'L3_xcond_b_m1': _L3_xcond_in['b_m1'], 'L3_xcond_w_m2': _L3_xcond_in['w_m2'], 'L3_xcond_b_m2': _L3_xcond_in['b_m2']}

def reference(x, cond_1024, ctx_1024, L0_xcond_W_mod, L0_xcond_b_mod, L0_xcond_W_qkv, L0_xcond_b_qkv, L0_xcond_W_proj, L0_xcond_b_proj, L0_xcond_W_qc, L0_xcond_b_qc, L0_xcond_W_kvc, L0_xcond_b_kvc, L0_xcond_W_cproj, L0_xcond_b_cproj, L0_xcond_W_mlp1, L0_xcond_b_mlp1, L0_xcond_W_mlp2, L0_xcond_b_mlp2, L1_xcond_adaln_w, L1_xcond_adaln_b, L1_xcond_qkv_w, L1_xcond_qkv_b, L1_xcond_sa_proj_w, L1_xcond_sa_proj_b, L1_xcond_q_w, L1_xcond_q_b, L1_xcond_kv_w, L1_xcond_kv_b, L1_xcond_ca_proj_w, L1_xcond_ca_proj_b, L1_xcond_fc1_w, L1_xcond_fc1_b, L1_xcond_fc2_w, L1_xcond_fc2_b, L2_xcond_Wq, L2_xcond_bq, L2_xcond_Wkv, L2_xcond_bkv, L2_xcond_Wp, L2_xcond_bp, L2_xcond_Wss_q, L2_xcond_bss_q, L2_xcond_Wss_kv, L2_xcond_bss_kv, L3_xcond_w_ada, L3_xcond_b_ada, L3_xcond_w_qkv, L3_xcond_b_qkv, L3_xcond_w_so, L3_xcond_b_so, L3_xcond_w_q, L3_xcond_b_q, L3_xcond_w_kv, L3_xcond_b_kv, L3_xcond_w_co, L3_xcond_b_co, L3_xcond_w_m1, L3_xcond_b_m1, L3_xcond_w_m2, L3_xcond_b_m2):
    import jax
    import jax.numpy as jnp

    def _L0_xcond_ref(x, c, context, W_mod, b_mod, W_qkv, b_qkv, W_proj, b_proj, W_qc, b_qc, W_kvc, b_kvc, W_cproj, b_cproj, W_mlp1, b_mlp1, W_mlp2, b_mlp2):
        import jax, jax.numpy as jnp
        import numpy as np
        LN_EPS = 1e-06

        def _ln(x):
            mu = jnp.mean(x, axis=-1, keepdims=True)
            var = jnp.var(x, axis=-1, keepdims=True)
            return (x - mu) * jax.lax.rsqrt(var + LN_EPS)
        B, N, H = x.shape
        NH = 16
        hd = H // NH
        scale = hd ** (-0.5)
        c_proj = jax.nn.silu(c) @ W_mod + b_mod
        shift_a, scale_a, gate_a, shift_m, scale_m, gate_m = jnp.split(c_proj, 6, axis=-1)

        def modulate(t, shift, sc):
            return t * (1 + sc[:, None]) + shift[:, None]
        x_norm = modulate(_ln(x), shift_a, scale_a)
        qkv = x_norm @ W_qkv + b_qkv
        q, k, v = jnp.split(qkv, 3, axis=-1)
        q = q.reshape(B, N, NH, hd).transpose(0, 2, 1, 3)
        k = k.reshape(B, N, NH, hd).transpose(0, 2, 1, 3)
        v = v.reshape(B, N, NH, hd).transpose(0, 2, 1, 3)
        attn_w = jax.nn.softmax(jnp.einsum('bhqd,bhkd->bhqk', q, k) * scale, axis=-1)
        attn_out = jnp.einsum('bhqk,bhkd->bhqd', attn_w, v)
        attn_out = attn_out.transpose(0, 2, 1, 3).reshape(B, N, H)
        attn_out = attn_out @ W_proj + b_proj
        x = x + gate_a[:, None] * attn_out
        S = context.shape[1]
        q_c = _ln(x) @ W_qc + b_qc
        kv_c = _ln(context) @ W_kvc + b_kvc
        k_c, v_c = jnp.split(kv_c, 2, axis=-1)
        q_c = q_c.reshape(B, N, NH, hd).transpose(0, 2, 1, 3)
        k_c = k_c.reshape(B, S, NH, hd).transpose(0, 2, 1, 3)
        v_c = v_c.reshape(B, S, NH, hd).transpose(0, 2, 1, 3)
        c_attn_w = jax.nn.softmax(jnp.einsum('bhqd,bhsd->bhqs', q_c, k_c) * scale, axis=-1)
        c_attn_out = jnp.einsum('bhqs,bhsd->bhqd', c_attn_w, v_c)
        c_attn_out = c_attn_out.transpose(0, 2, 1, 3).reshape(B, N, H)
        c_attn_out = c_attn_out @ W_cproj + b_cproj
        x = x + c_attn_out
        x_norm2 = modulate(_ln(x), shift_m, scale_m)
        h = jax.nn.gelu(x_norm2 @ W_mlp1 + b_mlp1)
        h = h @ W_mlp2 + b_mlp2
        x = x + gate_m[:, None] * h
        return x

    def _L1_xcond_ref(x, t_emb, context, adaln_w, adaln_b, qkv_w, qkv_b, sa_proj_w, sa_proj_b, q_w, q_b, kv_w, kv_b, ca_proj_w, ca_proj_b, fc1_w, fc1_b, fc2_w, fc2_b):
        import jax, jax.numpy as jnp
        import numpy as np
        D = 128
        H = 16
        HD = D // H
        MLP = 4 * D
        EPS = 1e-06
        SCALE = HD ** (-0.5)

        def _p(key, shape, s=0.02):
            return jax.random.normal(key, shape, dtype=jnp.float32) * s

        def _ln(x):
            mu = jnp.mean(x, axis=-1, keepdims=True)
            var = jnp.var(x, axis=-1, keepdims=True)
            return (x - mu) * jax.lax.rsqrt(var + EPS)

        def _heads(t):
            B, L, _ = t.shape
            return t.reshape(B, L, H, HD).transpose(0, 2, 1, 3)

        def _attend(q, k, v):
            attn = jnp.einsum('bhnd,bhsd->bhns', q, k) * SCALE
            attn = jax.nn.softmax(attn, axis=-1)
            o = jnp.einsum('bhns,bhsd->bhnd', attn, v)
            B, _, N, _ = q.shape
            return o.transpose(0, 2, 1, 3).reshape(B, N, D)
        B, N, _ = x.shape
        S = context.shape[1]
        mod = jax.nn.silu(t_emb) @ adaln_w + adaln_b
        sh_sa, sc_sa, g_sa, sh_ff, sc_ff, g_ff = jnp.split(mod[:, None, :], 6, axis=-1)
        xm = _ln(x) * (1.0 + sc_sa) + sh_sa
        qkv = (xm @ qkv_w + qkv_b).reshape(B, N, 3, H, HD)
        q = qkv[:, :, 0].transpose(0, 2, 1, 3)
        k = qkv[:, :, 1].transpose(0, 2, 1, 3)
        v = qkv[:, :, 2].transpose(0, 2, 1, 3)
        x_sa = _attend(q, k, v) @ sa_proj_w + sa_proj_b
        x = x + g_sa * x_sa
        xn = _ln(x)
        q = _heads(xn @ q_w + q_b)
        kv = (context @ kv_w + kv_b).reshape(B, S, 2, H, HD)
        k = kv[:, :, 0].transpose(0, 2, 1, 3)
        v = kv[:, :, 1].transpose(0, 2, 1, 3)
        x_ca = _attend(q, k, v) @ ca_proj_w + ca_proj_b
        x = x + x_ca
        xm = _ln(x) * (1.0 + sc_ff) + sh_ff
        h = jax.nn.gelu(xm @ fc1_w + fc1_b, approximate=True)
        x_ff = h @ fc2_w + fc2_b
        x = x + g_ff * x_ff
        return x

    def _L2_xcond_ref(x_q, x_kv, t_vec, Wq, bq, Wkv, bkv, Wp, bp, Wss_q, bss_q, Wss_kv, bss_kv):
        import jax, jax.numpy as jnp
        import numpy as np
        EPS = 1e-05

        def _ada_ln(x, c, W_ss, b_ss):
            mu = jnp.mean(x, axis=-1, keepdims=True)
            var = jnp.mean((x - mu) ** 2, axis=-1, keepdims=True)
            h = (x - mu) / jnp.sqrt(var + EPS)
            ss = jax.nn.silu(c) @ W_ss + b_ss
            scale, bias = jnp.split(ss, 2, axis=-1)
            return (1.0 + scale)[:, None, :] * h + bias[:, None, :]
        B, Lq, H = x_q.shape
        Lkv = x_kv.shape[1]
        nh = 16
        dh = H // nh
        xq = _ada_ln(x_q, t_vec, Wss_q, bss_q)
        xkv = _ada_ln(x_kv, t_vec, Wss_kv, bss_kv)
        q = (xq @ Wq + bq).reshape(B, Lq, nh, dh)
        kv = (xkv @ Wkv + bkv).reshape(B, Lkv, 2, nh, dh)
        k = kv[:, :, 0]
        v = kv[:, :, 1]
        scores = jnp.einsum('bqhd,bkhd->bhqk', q, k) / jnp.sqrt(jnp.float32(dh))
        attn = jax.nn.softmax(scores, axis=-1)
        out = jnp.einsum('bhqk,bkhd->bqhd', attn, v).reshape(B, Lq, H)
        return x_q + (out @ Wp + bp)

    def _L3_xcond_ref(x, mod, context, w_ada, b_ada, w_qkv, b_qkv, w_so, b_so, w_q, b_q, w_kv, b_kv, w_co, b_co, w_m1, b_m1, w_m2, b_m2):
        import jax, jax.numpy as jnp
        import numpy as np
        C = 128
        H = 16
        D = C // H
        WIN = 64
        SHIFT = 32
        TOPK = 16
        HID = 512
        EPS = 1e-06

        def _ln(x):
            x32 = x.astype(jnp.float32)
            m = x32.mean(-1, keepdims=True)
            v = jnp.mean((x32 - m) ** 2, axis=-1, keepdims=True)
            return ((x32 - m) * jax.lax.rsqrt(v + EPS)).astype(x.dtype)

        def _self_attn(h, w_qkv, b_qkv, w_so, b_so):
            B, L, _ = h.shape
            qkv = h @ w_qkv + b_qkv
            qkv = jnp.roll(qkv, -SHIFT, axis=1)
            nw = L // WIN
            qkv = qkv.reshape(B, nw, WIN, 3, H, D)
            q, k, v = (qkv[:, :, :, 0], qkv[:, :, :, 1], qkv[:, :, :, 2])
            scores = jnp.einsum('bnqhd,bnkhd->bnhqk', q, k) / jnp.sqrt(jnp.float32(D)).astype(h.dtype)
            attn = jax.nn.softmax(scores, axis=-1)
            o = jnp.einsum('bnhqk,bnkhd->bnqhd', attn, v).reshape(B, L, C)
            o = jnp.roll(o, SHIFT, axis=1)
            return o @ w_so + b_so

        def _topk_cross_attn(h, ctx, w_q, b_q, w_kv, b_kv, w_co, b_co):
            B, L, _ = h.shape
            Lc = ctx.shape[1]
            q = (h @ w_q + b_q).reshape(B, L, H, D)
            kv = (ctx @ w_kv + b_kv).reshape(B, Lc, 2, H, D)
            k, v = (kv[:, :, 0], kv[:, :, 1])
            scores = jnp.einsum('bqhd,bkhd->bhqk', q, k) / jnp.sqrt(jnp.float32(D)).astype(h.dtype)
            top_s, top_i = jax.lax.top_k(scores, TOPK)
            attn = jax.nn.softmax(top_s, axis=-1)
            v_bh = jnp.transpose(v, (0, 2, 1, 3))
            vg = jnp.take_along_axis(v_bh[:, :, None, :, :], top_i[..., None], axis=3)
            o = jnp.einsum('bhqk,bhqkd->bqhd', attn, vg).reshape(B, L, C)
            return o @ w_co + b_co

        def _swiglu(h, w_m1, b_m1, w_m2, b_m2):
            u = h @ w_m1 + b_m1
            a, b = (u[..., :HID], u[..., HID:])
            return jax.nn.silu(a) * b @ w_m2 + b_m2
        m = jax.nn.silu(mod) @ w_ada + b_ada
        sh_msa, sc_msa, g_msa, sh_mca, sc_mca, g_mca, sh_mlp, sc_mlp, g_mlp = [m[:, i * C:(i + 1) * C][:, None, :] for i in range(9)]
        h = _ln(x) * (1 + sc_msa) + sh_msa
        h = _self_attn(h, w_qkv, b_qkv, w_so, b_so)
        x = x + h * g_msa
        h = _ln(x) * (1 + sc_mca) + sh_mca
        h = _topk_cross_attn(h, context, w_q, b_q, w_kv, b_kv, w_co, b_co)
        x = x + h * g_mca
        h = _ln(x) * (1 + sc_mlp) + sh_mlp
        h = _swiglu(h, w_m1, b_m1, w_m2, b_m2)
        x = x + h * g_mlp
        return x
    x = _L0_xcond_ref(x, cond_1024, ctx_1024, L0_xcond_W_mod, L0_xcond_b_mod, L0_xcond_W_qkv, L0_xcond_b_qkv, L0_xcond_W_proj, L0_xcond_b_proj, L0_xcond_W_qc, L0_xcond_b_qc, L0_xcond_W_kvc, L0_xcond_b_kvc, L0_xcond_W_cproj, L0_xcond_b_cproj, L0_xcond_W_mlp1, L0_xcond_b_mlp1, L0_xcond_W_mlp2, L0_xcond_b_mlp2)
    x = _L1_xcond_ref(x, cond_1024, ctx_1024, L1_xcond_adaln_w, L1_xcond_adaln_b, L1_xcond_qkv_w, L1_xcond_qkv_b, L1_xcond_sa_proj_w, L1_xcond_sa_proj_b, L1_xcond_q_w, L1_xcond_q_b, L1_xcond_kv_w, L1_xcond_kv_b, L1_xcond_ca_proj_w, L1_xcond_ca_proj_b, L1_xcond_fc1_w, L1_xcond_fc1_b, L1_xcond_fc2_w, L1_xcond_fc2_b)
    x = _L2_xcond_ref(x, ctx_1024, cond_1024, L2_xcond_Wq, L2_xcond_bq, L2_xcond_Wkv, L2_xcond_bkv, L2_xcond_Wp, L2_xcond_bp, L2_xcond_Wss_q, L2_xcond_bss_q, L2_xcond_Wss_kv, L2_xcond_bss_kv)
    x = _L3_xcond_ref(x, cond_1024, ctx_1024, L3_xcond_w_ada, L3_xcond_b_ada, L3_xcond_w_qkv, L3_xcond_b_qkv, L3_xcond_w_so, L3_xcond_b_so, L3_xcond_w_q, L3_xcond_b_q, L3_xcond_w_kv, L3_xcond_b_kv, L3_xcond_w_co, L3_xcond_b_co, L3_xcond_w_m1, L3_xcond_b_m1, L3_xcond_w_m2, L3_xcond_b_m2)
    return x

_drawn_inputs = setup_inputs


def setup_inputs(seed=0):
    import zlib

    import numpy as np

    out = dict(_drawn_inputs(seed))
    spreads = {'L0_xcond_b_mod': (0.0, 0.1),
     'L0_xcond_b_qkv': (0.0, 0.1),
     'L0_xcond_b_proj': (0.0, 0.1),
     'L0_xcond_b_qc': (0.0, 0.508),
     'L0_xcond_b_kvc': (0.0, 0.1),
     'L0_xcond_b_cproj': (0.0, 0.1),
     'L0_xcond_b_mlp1': (0.0, 0.1),
     'L0_xcond_b_mlp2': (0.0, 0.1),
     'L2_xcond_bq': (0.0, 2.0),
     'L2_xcond_bkv': (0.0, 2.0),
     'L2_xcond_bp': (0.0, 0.8),
     'L2_xcond_bss_q': (0.0, 2.0),
     'L2_xcond_bss_kv': (0.0, 2.0),
     'L3_xcond_b_ada': (0.0, 0.6),
     'L3_xcond_b_qkv': (0.0, 0.8),
     'L3_xcond_b_so': (0.0, 0.522),
     'L3_xcond_b_q': (0.0, 0.8),
     'L3_xcond_b_kv': (0.0, 0.8),
     'L3_xcond_b_co': (0.0, 0.58),
     'L3_xcond_b_m1': (0.0, 0.8),
     'L3_xcond_b_m2': (0.0, 2.0)}
    factors = {'L1_xcond_adaln_w': 7.787,
     'L1_xcond_adaln_b': 8.0,
     'L1_xcond_qkv_w': 8.0,
     'L1_xcond_qkv_b': 8.0,
     'L1_xcond_sa_proj_w': 8.0,
     'L1_xcond_sa_proj_b': 8.0,
     'L1_xcond_q_w': 27.239,
     'L1_xcond_q_b': 193.757,
     'L1_xcond_kv_w': 2.957,
     'L1_xcond_kv_b': 28.988,
     'L1_xcond_ca_proj_w': 2.891,
     'L1_xcond_ca_proj_b': 17.562,
     'L1_xcond_fc1_w': 8.0,
     'L1_xcond_fc1_b': 8.0,
     'L1_xcond_fc2_w': 8.0,
     'L1_xcond_fc2_b': 26.465,
     'L2_xcond_Wq': 34.49,
     'L2_xcond_Wkv': 2.699,
     'L2_xcond_Wss_q': 45.38,
     'L2_xcond_Wss_kv': 24.456,
     'L3_xcond_w_qkv': 8.0,
     'L3_xcond_w_so': 8.0,
     'L3_xcond_w_q': 8.0,
     'L3_xcond_w_kv': 8.0,
     'L3_xcond_w_co': 8.0,
     'L3_xcond_w_m1': 8.0,
     'L3_xcond_w_m2': 8.0}
    for name, (base, spread) in spreads.items():
        noise = np.random.default_rng([zlib.crc32(name.encode()), seed]).standard_normal(out[name].shape)
        drawn = base * np.exp(spread * noise) if base else spread * noise
        out[name] = jnp.asarray(drawn.astype(out[name].dtype))
    for name, factor in factors.items():
        out[name] = (out[name] * factor).astype(out[name].dtype)
    return out
```

```python
from contextlib import ExitStack

import numpy as np

import concourse.bass as bass
from concourse import mybir

ALU = mybir.AluOpType
ACT = mybir.ActivationFunctionType
AX_X = mybir.AxisListType.X
F32 = mybir.dt.float32
F32R = mybir.dt.float32r

B, N, D = 4, 256, 128
NH, HD = 16, 8
P = 128
NT = N // P
HID = 4 * D
WIN, SHIFT = 64, 32
SCALE = float(HD) ** -0.5
FAR = 2.0 ** 100
GONE = 2.0 ** 127

MAX_ROW = 3 * HD
WIN_ROW = MAX_ROW + 2

WEIGHTS = [
    ("L0_xcond_W_mod", 6), ("L0_xcond_W_qkv", 3), ("L0_xcond_W_proj", 1), ("L0_xcond_W_qc", 1),
    ("L0_xcond_W_kvc", 2), ("L0_xcond_W_cproj", 1), ("L0_xcond_W_mlp1", 4), ("L0_xcond_W_mlp2", 4),
    ("L1_xcond_adaln_w", 6), ("L1_xcond_qkv_w", 3), ("L1_xcond_sa_proj_w", 1), ("L1_xcond_q_w", 1),
    ("L1_xcond_kv_w", 2), ("L1_xcond_ca_proj_w", 1), ("L1_xcond_fc1_w", 4), ("L1_xcond_fc2_w", 4),
    ("L2_xcond_Wss_q", 2), ("L2_xcond_Wss_kv", 2), ("L2_xcond_Wq", 1), ("L2_xcond_Wkv", 2),
    ("L2_xcond_Wp", 1),
    ("L3_xcond_w_ada", 9), ("L3_xcond_w_qkv", 3), ("L3_xcond_w_so", 1), ("L3_xcond_w_q", 1),
    ("L3_xcond_w_kv", 2), ("L3_xcond_w_co", 1), ("L3_xcond_w_m1", 8), ("L3_xcond_w_m2", 4),
]
WAT = {}
_n = 0
for _name, _k in WEIGHTS:
    WAT[_name] = _n
    _n += _k
NW = _n
WGROUPS = [0, WAT["L0_xcond_W_proj"], WAT["L1_xcond_adaln_w"], WAT["L2_xcond_Wss_q"], NW]

ROW_BIASES = [
    ("L0_xcond_b_mod", 2, 1), ("L0_xcond_b_mod", 5, 1), ("L1_xcond_adaln_b", 2, 1),
    ("L1_xcond_adaln_b", 5, 1), ("L3_xcond_b_ada", 2, 1), ("L3_xcond_b_ada", 5, 1),
    ("L3_xcond_b_ada", 8, 1),
    ("L0_xcond_b_qkv", 2, 1), ("L0_xcond_b_kvc", 1, 1), ("L1_xcond_qkv_b", 2, 1),
    ("L1_xcond_kv_b", 1, 1), ("L2_xcond_bkv", 1, 1), ("L3_xcond_b_qkv", 2, 1), ("L3_xcond_b_kv", 1, 1),
    ("L0_xcond_b_proj", 0, 1), ("L0_xcond_b_cproj", 0, 1), ("L1_xcond_sa_proj_b", 0, 1),
    ("L1_xcond_ca_proj_b", 0, 1), ("L2_xcond_bp", 0, 1), ("L3_xcond_b_so", 0, 1),
    ("L3_xcond_b_co", 0, 1),
    ("L0_xcond_b_mlp2", 0, 1), ("L1_xcond_fc2_b", 0, 1), ("L3_xcond_b_m2", 0, 1),
]
GATE_B, V_B, PROJ_B, DOWN_B = 0, 7, 14, 21

MODS = [
    ("L0_xcond_W_mod", "L0_xcond_b_mod", [1, 4], [0, 3], [2, 5]),
    ("L1_xcond_adaln_w", "L1_xcond_adaln_b", [1, 4], [0, 3], [2, 5]),
    ("L2_xcond_Wss_q", "L2_xcond_bss_q", [0], [1], []),
    ("L2_xcond_Wss_kv", "L2_xcond_bss_kv", [0], [1], []),
    ("L3_xcond_w_ada", "L3_xcond_b_ada", [1, 4, 7], [0, 3, 6], [2, 5, 8]),
]
MOD_AT = np.cumsum([0] + [len(m[2]) + len(m[3]) for m in MODS]).tolist()
GATE_AT = np.cumsum([0] + [len(m[4]) for m in MODS]).tolist()
COL_BIASES = [(m[1], j, 1) for m in MODS for j in m[2] + m[3]]
Q_B = len(COL_BIASES)
COL_BIASES += [("L0_xcond_b_qkv", 0, 1), ("L0_xcond_b_qc", 0, 1), ("L1_xcond_qkv_b", 0, 1),
               ("L1_xcond_q_b", 0, 1), ("L2_xcond_bq", 0, 1), ("L3_xcond_b_qkv", 0, 1),
               ("L3_xcond_b_q", 0, 1)]
K_B = len(COL_BIASES)
COL_BIASES += [("L0_xcond_b_qkv", 1, 1), ("L0_xcond_b_kvc", 0, 1), ("L1_xcond_qkv_b", 1, 1),
               ("L1_xcond_kv_b", 0, 1), ("L2_xcond_bkv", 0, 1), ("L3_xcond_b_qkv", 1, 1),
               ("L3_xcond_b_kv", 0, 1)]
UP_B = len(COL_BIASES)
COL_BIASES += [("L0_xcond_b_mlp1", 0, 4), ("L1_xcond_fc1_b", 0, 4), ("L3_xcond_b_m1", 0, 8)]
NCOL = sum(k for _, _, k in COL_BIASES)

def _mod(m, j):
    return MOD_AT[m] + j, MOD_AT[m] + len(MODS[m][2]) + j


ATTN = [
    dict(q=WAT["L0_xcond_W_qkv"], k=WAT["L0_xcond_W_qkv"] + 1, v=WAT["L0_xcond_W_qkv"] + 2,
         o=WAT["L0_xcond_W_proj"], kv="x", mod=_mod(0, 0), eps=1e-6, gate=GATE_AT[0], kind="full"),
    dict(q=WAT["L0_xcond_W_qc"], k=WAT["L0_xcond_W_kvc"], v=WAT["L0_xcond_W_kvc"] + 1,
         o=WAT["L0_xcond_W_cproj"], kv="ctx_norm", mod=None, cmod=None, eps=1e-6, gate=None, kind="full"),
    dict(q=WAT["L1_xcond_qkv_w"], k=WAT["L1_xcond_qkv_w"] + 1, v=WAT["L1_xcond_qkv_w"] + 2,
         o=WAT["L1_xcond_sa_proj_w"], kv="x", mod=_mod(1, 0), eps=1e-6, gate=GATE_AT[1], kind="full"),
    dict(q=WAT["L1_xcond_q_w"], k=WAT["L1_xcond_kv_w"], v=WAT["L1_xcond_kv_w"] + 1,
         o=WAT["L1_xcond_ca_proj_w"], kv="ctx", mod=None, eps=1e-6, gate=None, kind="full"),
    dict(q=WAT["L2_xcond_Wq"], k=WAT["L2_xcond_Wkv"], v=WAT["L2_xcond_Wkv"] + 1,
         o=WAT["L2_xcond_Wp"], kv="ctx_norm", mod=_mod(2, 0), cmod=_mod(3, 0), eps=1e-5, gate=None,
         kind="full"),
    dict(q=WAT["L3_xcond_w_qkv"], k=WAT["L3_xcond_w_qkv"] + 1, v=WAT["L3_xcond_w_qkv"] + 2,
         o=WAT["L3_xcond_w_so"], kv="x", mod=_mod(4, 0), eps=1e-6, gate=GATE_AT[4], kind="window"),
    dict(q=WAT["L3_xcond_w_q"], k=WAT["L3_xcond_w_kv"], v=WAT["L3_xcond_w_kv"] + 1,
         o=WAT["L3_xcond_w_co"], kv="ctx", mod=_mod(4, 1), eps=1e-6, gate=GATE_AT[4] + 1, kind="topk"),
]
MLP = [
    dict(up=WAT["L0_xcond_W_mlp1"], down=WAT["L0_xcond_W_mlp2"], mod=_mod(0, 1), eps=1e-6,
         gate=GATE_AT[0] + 1, bias=UP_B, act="gelu"),
    dict(up=WAT["L1_xcond_fc1_w"], down=WAT["L1_xcond_fc2_w"], mod=_mod(1, 1), eps=1e-6,
         gate=GATE_AT[1] + 1, bias=UP_B + 4, act="gelu"),
    dict(up=WAT["L3_xcond_w_m1"], down=WAT["L3_xcond_w_m2"], mod=_mod(4, 2), eps=1e-6,
         gate=GATE_AT[4] + 2, bias=UP_B + 8, act="swiglu"),
]
BLOCK_OF_ATTN = [0, 0, 1, 1, 2, 4, 4]
def norm_of(l):
    if l < 7:
        a = ATTN[l]
        return "x", a["mod"], a["eps"]
    if l < 10:
        return "x", MLP[l - 7]["mod"], MLP[l - 7]["eps"]
    return "ctx", ATTN[l - 10]["cmod"], ATTN[l - 10]["eps"]


COST = {
    "mods": [("pe", 1100), ("dve", 350)],
    "gates": [("pe", 500), ("dve", 1260)],
    "context": [("pe", 250), ("act", 2160)],
    "stats": [("dve", 765), ("pool", 800)],
    "normed": [("dve", 500), ("pe", 250), ("act", 500)],
    "qk": [("pe", 900), ("act", 1140), ("pool", 2000)],
    "values": [("pe", 130), ("dve", 630)],
    "stack_q": [("pe", 900), ("act", 475)],
    "stack_k": [("pe", 900), ("dve", 1200)],
    "scores": [("pe", 220), ("dve", 600)],
    "maxima": [("dve", 350), ("pe", 216), ("act", 350), ("dma", 4500)],
    "weights": [("pe", 440), ("act", 920)],
    "topk": [("pe", 220), ("dve", 2380), ("act", 1959), ("pool", 909)],
    "turned": [("pe", 867), ("act", 382)],
    "mix": [("pe", 1000), ("act", 400)],
    "divide": [("pe", 420), ("dve", 700)],
    "heads_out": [("pe", 200), ("act", 480)],
    "residual": [("pe", 450), ("dve", 1080)],
    "up": [("pe", 624), ("act", 2900)],
    "up_gate": [("pe", 1750), ("dve", 4080)],
    "down": [("pe", 1750), ("dve", 1800)],
}
PSUM_RING = {"mods": "misc", "gates": "misc", "context": "misc", "normed": "misc", "qk": "misc",
             "values": "misc", "maxima": "misc", "divide": "misc", "heads_out": "misc",
             "residual": "misc", "down": "misc", "mix": "misc", "stack_q": "wide", "stack_k": "wide",
             "weights": "wide", "turned": "wide", "up": "wide", "up_gate": "wide",
             "scores": "score", "topk": "score"}
SLOTS = {"misc": 2, "wide": 2, "score": 2}
READER = {"mods": "dve", "gates": "dve", "context": "act", "normed": "act", "qk": "act",
          "values": "dve", "maxima": "act", "divide": "dve", "heads_out": "act", "residual": "dve",
          "down": "dve", "stack_q": "act", "stack_k": "dve", "weights": "act", "turned": "act",
          "up": "act", "up_gate": "dve", "scores": "dve", "topk": "act", "mix": "act"}


def attention_steps(b, l):
    a = ATTN[l]
    yield "stats", b, l, 0
    if a["kv"] == "ctx_norm":
        yield "stats", b, 10 + l, 0
    yield "normed", b, l, 0
    if a["kv"] == "ctx_norm":
        yield "normed", b, 10 + l, 0
    yield "qk", b, l, 0
    yield "values", b, l, 0
    yield "stack_k", b, l, 0
    yield "stack_q", b, l, 0
    if a["kind"] == "topk":
        for i in range(NH):
            yield "topk", b, l, i
            if i % 2 and i > 2:
                yield "turned", b, l, i // 2 - 1
                if i % 4 == 1:
                    yield from mix_steps(b, l, i // 4 - 1)
        yield "turned", b, l, 7
        yield from mix_steps(b, l, 3)
    else:
        for i in range(NH):
            yield "scores", b, l, i
        yield "maxima", b, l, 0
        for u in range(8):
            yield "weights", b, l, u
            if u and u % 2 == 0:
                yield from mix_steps(b, l, u // 2 - 1)
        yield from mix_steps(b, l, 3)
    yield "heads_out", b, l, 0
    yield "residual", b, l, 0


def mix_steps(b, l, s):
    yield "mix", b, l, s
    if s % 2:
        yield "divide", b, l, s // 2


def mlp_steps(b, l):
    yield "stats", b, 7 + l, 0
    yield "normed", b, 7 + l, 0
    yield "up", b, l, 0
    if MLP[l]["act"] == "swiglu":
        yield "up_gate", b, l, 0
    yield "down", b, l, 0


def batch_steps(b):
    yield "context", b, 0, 0
    for what, l in (("a", 0), ("a", 1), ("m", 0), ("a", 2), ("a", 3), ("m", 1), ("a", 4), ("a", 5),
                    ("a", 6), ("m", 2)):
        yield from (attention_steps if what == "a" else mlp_steps)(b, l)


def needs(step):
    kind, b, l, u = step
    if kind in ("scores", "topk"):
        return [("stack_k", b, l, 0), ("stack_q", b, l, 0)]
    if kind == "weights":
        return [("maxima", b, l, 0)]
    if kind == "turned":
        return [("topk", b, l, 2 * u + 1)]
    if kind == "mix":
        return [("turned" if ATTN[l]["kind"] == "topk" else "weights", b, l, 2 * u + 1)]
    if kind == "divide":
        return [("mix", b, l, 2 * u + 1)]
    if kind == "heads_out":
        return [("divide", b, l, 1)]
    if kind == "stack_q" or kind == "stack_k" or kind == "values":
        return [("qk", b, l, 0)]
    return None


def interleave():
    chains = [list(batch_steps(b)) for b in range(B)]
    at = [0] * B
    free = dict.fromkeys(("pe", "act", "dve", "pool", "dma"), 0.0)
    ended, started = {}, {}
    ring = {r: [0.0] * n for r, n in SLOTS.items()}
    order = []
    block = 0
    stacking = [0]
    softmaxes, halves = [PT_SLOTS], [0]

    def run(step, t):
        kind = step[0]
        slot = None
        if kind in ("weights", "turned"):
            softmaxes[0] -= 1
            halves[0] += 1 if step[3] % 2 == 0 else -1
        if kind == "mix":
            softmaxes[0] += 2
        if kind == "qk":
            stacking[0] += 1
        if kind == "stack_q":
            stacking[0] -= 1
        if kind in PSUM_RING:
            slot = ring[PSUM_RING[kind]]
            t = max(t, slot.pop(0))
        begun = None
        for eng, ns in COST[kind]:
            t = max(t, free[eng] if eng != "dma" else 0.0)
            begun = t if begun is None else begun
            t += ns
            if eng != "dma":
                free[eng] = t
            if slot is not None and eng == READER[kind]:
                slot.append(t)
            t += HOP
        started[step], ended[step] = begun, t
        order.append(step)

    def begin(step, prev):
        need = needs(step)
        if need is None:
            t = ended.get(prev, 0.0)
        else:
            t = max(ended[n] for n in need)
            t = max(t, started.get(prev, 0.0))
        kind = step[0]
        if kind in PSUM_RING:
            t = max(t, ring[PSUM_RING[kind]][0])
        if kind in ("weights", "turned"):
            if softmaxes[0] < (1 if step[3] % 2 else 2 + halves[0]):
                return float("inf")
        if kind == "qk" and stacking[0] == 2:
            return float("inf")
        first = COST[kind][0][0]
        return max(t, free[first])

    def wasted(step, t):
        idle = 0.0
        for n, (eng, ns) in enumerate(COST[step[0]]):
            if eng != "dma":
                if n and t > free[eng]:
                    idle += min(t - free[eng], 5000.0)
                t = max(t, free[eng])
            t += ns + HOP
        return idle

    for m in range(len(MODS)):
        if m == 0:
            run(("mods", 0, m, 0), 0.0)
            for b in range(B):
                run(("gates", b, m, 0), 0.0)
            block = 1
    while any(at[b] < len(chains[b]) for b in range(B)):
        best = None
        for b in range(B):
            if at[b] == len(chains[b]):
                continue
            step = chains[b][at[b]]
            prev = chains[b][at[b] - 1] if at[b] else None
            t = begin(step, prev)
            if t == float("inf") and step[0] == "weights" and chains[b][at[b] + 1][0] == "mix":
                chains[b][at[b]], chains[b][at[b] + 1] = chains[b][at[b] + 1], step
                step = chains[b][at[b]]
                t = begin(step, prev)
            key = (t + WASTE * wasted(step, t) + STAGGER * b - (BURST if order and order[-1][1] == b else 0.0), b)
            if best is None or key < best[0]:
                best = (key, t, b, step)
        _, t, b, step = best
        assert t < float("inf")
        if step[0] == "stats" and step[2] < 7:
            while block <= BLOCK_OF_ATTN[step[2]] or (step[2] == 4 and block <= 3):
                run(("mods", 0, block, 0), 0.0)
                if MODS[block][4]:
                    for g in range(B):
                        run(("gates", g, block, 0), 0.0)
                block += 1
        run(step, t)
        at[b] += 1
    return order


STAGGER = 32.3
PT_SLOTS = 4
BURST = 99.1
WASTE = 0.0
HOP = 100.0
ORDER = interleave()
ORDINAL, _seen = {}, {}
for _s in ORDER:
    _seen[_s[0]] = _seen.get(_s[0], 0) + 1
    ORDINAL[_s] = _seen[_s[0]]
SLOT, HAD = {}, {}
_users = {r: [] for r in SLOTS}
for _s in ORDER:
    if _s[0] in PSUM_RING:
        _r = PSUM_RING[_s[0]]
        SLOT[_s] = len(_users[_r]) % SLOTS[_r]
        HAD[_s] = _users[_r][-SLOTS[_r]] if len(_users[_r]) >= SLOTS[_r] else None
        _users[_r].append(_s)
PT_SLOT, PT_HAD, _pt = {}, {}, [(n, None) for n in range(PT_SLOTS)]
QK_SLOTS = 2
_qk = [s for s in ORDER if s[0] == "qk"]
QK_SLOT = {s[1:]: n % QK_SLOTS for n, s in enumerate(_qk)}
QK_HAD = {s: _qk[n - QK_SLOTS] if n >= QK_SLOTS else None for n, s in enumerate(_qk)}
TK_SLOTS = 2
TK_SLOT, TK_HAD, _tk = {}, {}, []
SEL_SLOTS = 4
SEL_SLOT, SEL_HAD = {}, {}
for _s in ORDER:
    if _s[0] in ("weights", "turned"):
        PT_SLOT[_s[1:]], PT_HAD[_s] = _pt.pop(0)
    if _s[0] == "mix":
        for _u in (2 * _s[3], 2 * _s[3] + 1):
            _pt.append((PT_SLOT[_s[1], _s[2], _u], _s))
    if _s[0] == "topk":
        TK_SLOT[_s] = len(_tk) % TK_SLOTS
        TK_HAD[_s] = _tk[-TK_SLOTS] if len(_tk) >= TK_SLOTS else None
        SEL_SLOT[_s] = len(_tk) % SEL_SLOTS
        _h = _tk[-SEL_SLOTS] if len(_tk) >= SEL_SLOTS else None
        SEL_HAD[_s] = ("turned", _h[1], _h[2], _h[3] // 2) if _h else None
        _tk.append(_s)
X_FROM, _last = {}, {}
for _s in ORDER:
    if _s[0] == "stats":
        X_FROM[_s] = _last.get(_s[1]) if _s[2] < 10 else None
    if _s[0] in ("residual", "down"):
        _last[_s[1]] = _s
WINDOW_NTH = {s[1]: n + 1 for n, s in enumerate(s for s in ORDER if s[0] == "scores" and s[3] == 0 and ATTN[s[2]]["kind"] == "window")}
def head_of(i):
    s, g = i // 4, i % 4
    return s, g, 4 * g + s


def constants():
    sel = np.zeros((P, 2, 2, 4, P), np.float32)
    for g in range(4):
        for s in range(4):
            for d in range(HD):
                row = HD * (4 * g + s) + d
                for t in range(3):
                    sel[row, 0, (0, 0, 1)[t], s, 32 * g + HD * t + d] = 1.0
                    sel[row, 1, (0, 1, 0)[t], s, 32 * g + HD * t + d] = 1.0
    win = np.arange(N) // WIN
    masks = np.zeros((P, 2, N), np.float32)
    ones = np.zeros((P, 1), np.float32)
    for g in range(4):
        ones[32 * g + MAX_ROW:32 * g + MAX_ROW + 2] = 1.0
        for w in range(N // WIN):
            masks[32 * g + WIN_ROW + w, 0] = win != w
            masks[32 * g + WIN_ROW + w, 1] = -FAR * (win == w)
    return {
        "select": sel.reshape(P, -1), "window_rows": masks.reshape(P, -1), "max_rows": ones,
        "identity": np.eye(P, dtype=np.float32), "half_power": np.full((P, 4), -0.5, np.float32),
    }


def build(nc, x_in, cond, ctx_in, w_in, rows_in, cols_in, c_select, c_window, c_maxrows, c_ident,
          c_pow, out):
    with ExitStack() as es:
        def sb(name, shape, dt=F32):
            return es.enter_context(nc.sbuf_tensor(name, shape, dt))

        def sem(name):
            return es.enter_context(nc.semaphore(name))

        w = sb("weights", [P, NW, D])
        row_b = sb("row_biases", [P, len(ROW_BIASES), D])
        col_b = sb("column_biases", [P, NCOL])
        ident = sb("identity", [P, P])
        sel = sb("select", [P, 2, 2, 4, P], F32R)
        win_rows = sb("window_rows", [P, 2, N])
        max_rows = sb("max_rows", [P, 1])
        half_pow = sb("half_power", [P, 4])
        x = sb("x", [P, B, NT, D])
        ctx = sb("context", [P, B, NT, D])
        cT = sb("cond_T", [P, B])
        cTanh = sb("cond_tanh", [P, B])
        cSilu = sb("cond_silu", [P, B])
        cWide = sb("cond_silu_wide", [P, B, P])
        mod = sb("modulations", [P, MOD_AT[-1], B])
        gate = sb("gates", [P, B, GATE_AT[-1], D])
        ctxT = sb("context_T", [P, B, N])
        stats = sb("stats", [P, B, NT, 6])
        mv = sb("mean_var", [P, B, 2, NT, 2])
        rstd = sb("rstd", [P, B, 2, NT])
        z = sb("centred", [P, B, NT, D])
        hT = sb("normed_T", [P, B, N])
        hcT = sb("context_normed_T", [P, B, N])
        qk = sb("qk", [P, 2, 2, N])
        hi = sb("qk_hi", [P, 2, 2, N], F32R)
        lo = sb("qk_lo", [P, 2, 2, N], F32R)
        QS = [sb(f"q_stack{b}", [P, 4, N], F32R) for b in range(B)]
        KS = [sb(f"k_stack{b}", [P, 4, N], F32R) for b in range(B)]
        VW = 9 * NH + 24
        V = sb("values", [P, B, NT, VW])
        negmax = sb("negmax", [P, B, 4, 4, NT])
        mhl = sb("negmax_halves", [P, B, 2, 4, 2, 4 * NT], F32R)
        mT = sb("negmax_T", [64, B, P])
        pT = sb("softmax_T", [P, PT_SLOTS, 4, N])
        mixT = sb("mixed_T", [P, B, 4, N])
        rden = sb("rden", [P, B, 2, NT, 4])
        top8 = sb("top8", [P, TK_SLOTS, NT, 2, 8])
        ntop = sb("neg_top", [P, TK_SLOTS, NT])
        left = sb("left", [P, TK_SLOTS, NT, N])
        ex = sb("exps", [P, TK_SLOTS, NT, N])
        picked = sb("picked", [P, SEL_SLOTS, NT, N])
        minus1 = sb("minus_one", [P, 1])

        wide = es.enter_context(nc.psum_tensor("wide", [P, 2, 4, N], F32))
        score = es.enter_context(nc.psum_tensor("score", [P, 2, NT, N], F32))
        misc2 = es.enter_context(nc.psum_tensor("misc", [P, 2, 512], F32))

        done = {(k, e): sem(f"{k}_{e}") for k, parts in COST.items() for e, _ in parts
                if e != "dma"}
        topk_scored = sem("topk_rows_read")
        topk_exped = sem("topk_exps")
        max_rows_in = [sem(f"max_rows_in{b}") for b in range(B)]
        s_in = sem("small_inputs")
        s_w = [sem(f"weights_in{i}") for i in range(len(WGROUPS) - 1)]
        s_x = sem("x_in")
        s_ctx = sem("context_in")
        s_out = sem("out_written")
        s_cond = sem("cond_chain")
        s_init = sem("initial_values")
        s_dve = sem("dve_chain")
        s_act = sem("act_chain")
        s_pool = sem("pool_chain")
        window_q = sem("window_q_rows")
        block = es.enter_context(nc.Block())

        def after(eng, part, step):
            eng.wait_ge(done[step[0], part], ORDINAL[step])

        def bank_free(eng, step):
            if HAD[step] is not None:
                after(eng, READER[HAD[step][0]], HAD[step])

        def weights_in(eng, blk):
            for i in range(len(WGROUPS) - 1):
                if WGROUPS[i] <= blk < WGROUPS[i + 1]:
                    eng.wait_ge(s_w[i], 16)

        N_SMALL = 7

        @block.sync
        def _(sp):
            sp.dma_start(cT[:], cond).then_inc(s_in, 16)
            sp.dma_start(x[:], x_in.rearrange("b (t p) f -> p b t f", p=P)).then_inc(s_x, 16)
            sp.dma_start(w[:, WGROUPS[0]:WGROUPS[1], :], w_in[:, WGROUPS[0]:WGROUPS[1], :]).then_inc(s_w[0], 16)
            sp.dma_start(ctx[:], ctx_in.rearrange("b (t p) f -> p b t f", p=P)).then_inc(s_ctx, 16)
            sp.wait_ge(s_in, 16 * (N_SMALL + 1))
            for i in range(1, len(WGROUPS) - 1):
                sp.dma_start(w[:, WGROUPS[i]:WGROUPS[i + 1], :],
                             w_in[:, WGROUPS[i]:WGROUPS[i + 1], :]).then_inc(s_w[i], 16)
            for step in ORDER:
                kind, b, l, u = step
                if kind == "maxima":
                    after(sp, "act", step)
                    for g in range(4):
                        sp.dma_start(QS[b][32 * g + MAX_ROW:32 * g + MAX_ROW + 2, :, :].bitcast(F32),
                                     mT[16 * g:16 * g + 16, b, :]).then_inc(max_rows_in[b], 16)
                elif kind == "down" and l == 2:
                    after(sp, "dve", step)
                    sp.dma_start(out[b].rearrange("(t p) f -> p t f", p=P), x[:, b, :, :]).then_inc(s_out, 16)
            sp.wait_ge(s_out, 16 * B)

        @block.gpsimd
        def _(pool):
            chain = 0
            nc.gpsimd.memset(V[:], 0.0).then_inc(s_pool, 1)
            pool.wait_ge(s_pool, 1)
            nc.gpsimd.memset(V[:, :, :, 0:9 * NH].rearrange("p b t (h e) -> p (b t) h e", e=9)[:, :, :, HD:9],
                             1.0).then_inc(s_init, 1)
            nc.gpsimd.memset(minus1[:], -1.0).then_inc(s_init, 1)
            chain = 1
            pool.wait_ge(s_in, 16 * (N_SMALL + 1))
            pool.wait_ge(s_x, 16)
            for step in ORDER:
                kind, b, l, u = step
                if kind == "stats":
                    c = 0 if norm_of(l)[0] == "x" else 1
                    after(pool, "dve", step)
                    nc.gpsimd.tensor_tensor(rstd[:, b, c, :], mv[:, b, c, :, 1], half_pow[:, 0:NT],
                                            ALU.pow).then_inc(done[kind, "pool"], 1)
                elif kind == "qk":
                    slot = QK_SLOT[step[1:]]
                    after(pool, "act", step)
                    if QK_HAD[step] is not None:
                        after(pool, "pe", ("stack_q", *QK_HAD[step][1:]))
                    nc.gpsimd.tensor_tensor(lo[:, slot, :, :], qk[:, slot, :, :], hi[:, slot, :, :].bitcast(F32),
                                            ALU.subtract).then_inc(done[kind, "pool"], 1)
                elif kind == "topk":
                    k, p = TK_SLOT[step], SEL_SLOT[step]
                    after(pool, "act", step)
                    if SEL_HAD[step] is not None:
                        after(pool, "pe", SEL_HAD[step])
                    nc.gpsimd.tensor_tensor(picked[:, p, :, :], ex[:, k, :, :], left[:, k, :, :],
                                            ALU.mult).then_inc(done[kind, "pool"], 1)

        @block.scalar
        def _(act):
            act.dma_start(col_b[:], cols_in).then_inc(s_in, 16)
            act.dma_start(ident[:], c_ident).then_inc(s_in, 16)
            act.dma_start(row_b[:].rearrange("p a f -> p (a f)"), rows_in.partition_broadcast(P)).then_inc(s_in, 16)
            act.dma_start(mixT[:, 0:2, :, :].rearrange("p b s n -> p (b s n)"), c_select).then_inc(s_in, 16)
            act.dma_start(win_rows[:].rearrange("p a n -> p (a n)"), c_window).then_inc(s_in, 16)
            act.dma_start(max_rows[:], c_maxrows).then_inc(s_in, 16)
            act.dma_start(half_pow[:], c_pow).then_inc(s_in, 16)
            act.wait_ge(s_in, 16 * (N_SMALL + 1))
            nc.scalar.activation(cTanh[:], cT[:], ACT.Tanh, scale=0.5).then_inc(s_cond, 1)
            act.wait_ge(s_init, 4)
            for step in ORDER:
                kind, b, l, u = step
                fin = done.get((kind, "act"))
                misc = misc2[:, SLOT[step], :] if PSUM_RING.get(kind) == "misc" else None
                if kind == "context":
                    after(act, "pe", step)
                    nc.scalar.activation(ctxT[:, b, :], misc[:, 0:N], ACT.Copy).then_inc(fin, 1)
                elif kind == "normed":
                    what, m, _ = norm_of(l)
                    after(act, "pe", step)
                    dst = (hT if what == "x" else hcT)[:, b, :]
                    if l < 7 and ATTN[l]["kind"] == "window":
                        for to, at, n in ((0, SHIFT, N - SHIFT), (N - SHIFT, 0, SHIFT)):
                            ins = nc.scalar.activation(dst[:, to:to + n], misc[:, at:at + n], ACT.Identity,
                                                       scale=mod[:, m[0], b:b + 1], bias=mod[:, m[1], b:b + 1])
                        ins.then_inc(fin, 1)
                    elif m is None:
                        nc.scalar.activation(dst, misc[:, 0:N], ACT.Copy).then_inc(fin, 1)
                    else:
                        blk = max(i for i in range(len(MODS)) if MOD_AT[i] <= m[0])
                        after(act, "dve", ("mods", 0, blk, 0))
                        nc.scalar.activation(dst, misc[:, 0:N], ACT.Identity, scale=mod[:, m[0], b:b + 1],
                                             bias=mod[:, m[1], b:b + 1]).then_inc(fin, 1)
                elif kind == "qk":
                    slot = QK_SLOT[step[1:]]
                    after(act, "pe", step)
                    if QK_HAD[step] is not None:
                        after(act, "pool", QK_HAD[step])
                    act.wait_ge(s_cond, 4)
                    if QK_HAD[step] is not None:
                        after(act, "pe", ("stack_q", *QK_HAD[step][1:]))
                    nc.scalar.activation(hi[:, slot, 0, :], misc[:, 0:N], ACT.Identity, scale=SCALE,
                                         bias=col_b[:, Q_B + l:Q_B + l + 1])
                    nc.scalar.activation(hi[:, slot, 1, :], misc[:, N:2 * N], ACT.Identity,
                                         bias=col_b[:, K_B + l:K_B + l + 1])
                    nc.scalar.activation(qk[:, slot, 0, :], misc[:, 0:N], ACT.Identity, scale=SCALE,
                                         bias=col_b[:, Q_B + l:Q_B + l + 1]).then_inc(s_act, 1)
                    nc.scalar.activation(qk[:, slot, 1, :], misc[:, N:2 * N], ACT.Identity,
                                         bias=col_b[:, K_B + l:K_B + l + 1]).then_inc(fin, 1)
                elif kind == "stack_q":
                    after(act, "pe", step)
                    if ATTN[l]["kind"] == "window":
                        after(act, "dve", ("stack_k", b, l, 0))
                        nc.scalar.activation(QS[b][:, :, :], wide[:, SLOT[step], :, :], ACT.Copy).then_inc(fin, 1)
                    else:
                        nc.scalar.activation(QS[b][:, :, :], wide[:, SLOT[step], :, :], ACT.Copy).then_inc(fin, 1)
                elif kind == "maxima":
                    after(act, "pe", step)
                    nc.scalar.activation(mT[:, b, :], misc[0:64, 0:P], ACT.Copy).then_inc(fin, 1)
                elif kind in ("weights", "turned"):
                    after(act, "pe", step)
                    if PT_HAD[step] is not None:
                        after(act, "pe", PT_HAD[step])
                    cols = P if ATTN[l]["kind"] == "window" else N
                    nc.scalar.activation(pT[:, PT_SLOT[step[1:]], :, 0:cols], wide[:, SLOT[step], :, 0:cols],
                                         ACT.Exp if kind == "weights" else ACT.Copy).then_inc(fin, 1)
                elif kind == "topk":
                    k = TK_SLOT[step]
                    act.wait_ge(topk_scored, ORDINAL[step])
                    if TK_HAD[step] is not None:
                        after(act, "pool", TK_HAD[step])
                    for t in range(NT):
                        nc.scalar.activation(ex[:, k, t, :], score[:, SLOT[step], t, :], ACT.Exp,
                                             bias=ntop[:, k, t:t + 1]).then_inc(topk_exped, 1)
                    after(act, "dve", step)
                    nc.scalar.activation(left[:, k, :, :], left[:, k, :, :], ACT.Relu, scale=-2.0 / GONE,
                                         bias=minus1[:, 0:1]).then_inc(fin, 1)
                elif kind == "mix":
                    after(act, "pe", step)
                    nc.scalar.activation(mixT[:, b, u, :], misc[:, 0:N], ACT.Copy).then_inc(fin, 1)
                elif kind == "heads_out":
                    after(act, "pe", step)
                    if ATTN[l]["kind"] == "window":
                        for to, at, n in ((SHIFT, 0, N - SHIFT), (0, N - SHIFT, SHIFT)):
                            ins = nc.scalar.activation(hT[:, b, to:to + n], misc[:, at:at + n], ACT.Copy)
                        ins.then_inc(fin, 1)
                    else:
                        nc.scalar.activation(hT[:, b, :], misc[:, 0:N], ACT.Copy).then_inc(fin, 1)
                elif kind == "up":
                    after(act, "pe", step)
                    fn = ACT.Silu if MLP[l]["act"] == "swiglu" else ACT.Gelu_apprx_tanh
                    for j in range(4):
                        ins = nc.scalar.activation(mixT[:, b, j, :], wide[:, SLOT[step], j, :], fn,
                                                   bias=col_b[:, MLP[l]["bias"] + j:MLP[l]["bias"] + j + 1])
                    ins.then_inc(fin, 1)

        @block.vector
        def _(dve):
            chain = [0]

            def link(ins):
                chain[0] += 1
                ins.then_inc(s_dve, 1)
                dve.wait_ge(s_dve, chain[0])

            dve.wait_ge(s_in, 16 * (N_SMALL + 1))
            nc.vector.tensor_copy(sel[:].rearrange("p a h s c -> p (a h s c)"),
                                  mixT[:, 0:2, :, :].rearrange("p b s n -> p (b s n)")).then_inc(s_init, 1)
            nc.vector.memset(mhl[:].bitcast(F32), 0.0).then_inc(s_init, 1)
            nc.vector.tensor_scalar(col_b[:, Q_B:Q_B + 7], col_b[:, Q_B:Q_B + 7], SCALE, None,
                                    ALU.mult).then_inc(s_cond, 1)
            dve.wait_ge(s_cond, 2)
            link(nc.vector.tensor_scalar(cTanh[:], cTanh[:], 1.0, 0.5, ALU.add, ALU.mult))
            nc.vector.tensor_tensor(cSilu[:], cTanh[:], cT[:], ALU.mult).then_inc(s_cond, 1)
            dve.wait_ge(s_cond, 3)
            nc.vector.tensor_copy(cWide[:], cSilu[:].rearrange("p (b o) -> p b o", o=1).broadcast_to([P, B, P]))\
                .then_inc(s_cond, 1)
            dve.wait_ge(s_x, 16)
            dve.wait_ge(s_ctx, 16)
            dve.wait_ge(s_init, 4)
            for step in ORDER:
                kind, b, l, u = step
                fin = done.get((kind, "dve"))
                misc = misc2[:, SLOT[step], :] if PSUM_RING.get(kind) == "misc" else None
                if kind == "mods":
                    n = MOD_AT[l + 1] - MOD_AT[l]
                    cols = mod[:, MOD_AT[l]:MOD_AT[l + 1], :]
                    after(dve, "pe", step)
                    link(nc.vector.tensor_tensor(
                        cols, misc[:, 0:n * B].rearrange("p (n b) -> p n b", b=B),
                        col_b[:, MOD_AT[l]:MOD_AT[l + 1]].rearrange("p (n o) -> p n o", o=1).broadcast_to([P, n, B]),
                        ALU.add))
                    half = mod[:, MOD_AT[l]:MOD_AT[l] + n // 2, :]
                    nc.vector.tensor_scalar(half, half, 1.0, None, ALU.add).then_inc(fin, 1)
                elif kind == "gates":
                    n = GATE_AT[l + 1] - GATE_AT[l]
                    after(dve, "pe", step)
                    nc.vector.tensor_tensor(
                        gate[:, b, GATE_AT[l]:GATE_AT[l + 1], :],
                        misc[:, 0:n * D].rearrange("p (n f) -> p n f", f=D),
                        row_b[:, GATE_B + GATE_AT[l]:GATE_B + GATE_AT[l + 1], :], ALU.add).then_inc(fin, 1)
                elif kind == "stats":
                    what, _, eps = norm_of(l)
                    c = 0 if what == "x" else 1
                    src = x if what == "x" else ctx
                    if X_FROM[step] is not None:
                        after(dve, "dve", X_FROM[step])
                    for t in range(NT):
                        ins = nc.vector.bn_stats(stats[:, b, t, :], src[:, b, t, :])
                    link(ins)
                    for t in range(NT):
                        ins = nc.vector.bn_aggr(mv[:, b, c, t, :], stats[:, b, t, :])
                    link(ins)
                    nc.vector.tensor_scalar(mv[:, b, c, :, 1], mv[:, b, c, :, 1], eps, None,
                                            ALU.add).then_inc(fin, 1)
                elif kind == "normed":
                    c = 0 if norm_of(l)[0] == "x" else 1
                    src = x if c == 0 else ctx
                    after(dve, "pool", ("stats", b, l, 0))
                    if l >= 10:
                        after(dve, "pe", ("normed", b, l - 10, 0))
                    for t in range(NT):
                        ins = nc.vector.tensor_scalar(z[:, b, t, :], src[:, b, t, :], mv[:, b, c, t, 0:1],
                                                      rstd[:, b, c, t:t + 1], ALU.subtract, ALU.mult)
                    ins.then_inc(fin, 1)
                elif kind == "values":
                    after(dve, "pe", step)
                    for t in range(NT):
                        ins = nc.vector.tensor_tensor(
                            V[:, b, t, 0:9 * NH].rearrange("p (h e) -> p h e", e=9)[:, :, 0:HD],
                            misc[:, D * t:D * t + D].rearrange("p (h e) -> p h e", e=HD),
                            row_b[:, V_B + l, :].rearrange("p (h e) -> p h e", e=HD), ALU.add)
                    ins.then_inc(fin, 1)
                elif kind == "stack_k":
                    after(dve, "pe", step)
                    ps = wide[:, SLOT[step], :, :]
                    if ATTN[l]["kind"] == "window":
                        nc.vector.scalar_tensor_tensor(
                            KS[b][:, :, :], ps, max_rows[:, 0:1],
                            win_rows[:, 1:2, :].broadcast_to([P, 4, N]), ALU.add, ALU.add).then_inc(fin, 1)
                    else:
                        nc.vector.tensor_scalar(KS[b][:, :, :], ps, max_rows[:, 0:1], None,
                                                ALU.add).then_inc(fin, 1)
                elif kind == "scores":
                    s, g, h = head_of(u)
                    if u == 0 and ATTN[l]["kind"] == "window":
                        after(dve, "act", ("stack_q", b, l, 0))
                        nc.vector.tensor_tensor(QS[b][:, :, :], QS[b][:, :, :].bitcast(F32),
                                                win_rows[:, 0:1, :].broadcast_to([P, 4, N]),
                                                ALU.add).then_inc(window_q, 1)
                    after(dve, "pe", step)
                    cols = P if ATTN[l]["kind"] == "window" else N
                    nc.vector.tensor_reduce(negmax[:, b, g, s, :], score[:, SLOT[step], :, 0:cols], AX_X, ALU.max,
                                            negate=True).then_inc(fin, 1)
                elif kind == "maxima":
                    dve.wait_ge(done["scores", "dve"], ORDINAL["scores", b, l, NH - 1])
                    m = negmax[:, b, :, :, :].rearrange("p g s t -> p g (s t)")
                    link(nc.vector.tensor_copy(mhl[:, b, 0, :, 0, :], m))
                    nc.vector.tensor_tensor(mhl[:, b, 0, :, 1, :], m, mhl[:, b, 0, :, 0, :].bitcast(F32),
                                            ALU.subtract).then_inc(fin, 1)
                elif kind == "topk":
                    k = TK_SLOT[step]
                    ps = score[:, SLOT[step], :, :]
                    after(dve, "pe", step)
                    if TK_HAD[step] is not None:
                        after(dve, "pool", TK_HAD[step])
                    for t in range(NT):
                        ins = nc.vector.max(top8[:, k, t, 0, :], ps[:, t, :])
                    link(ins)
                    nc.vector.tensor_scalar(ntop[:, k, :], top8[:, k, :, 0, 0], -1.0, None, ALU.mult)
                    for t in range(NT):
                        ins = nc.vector.match_replace(left[:, k, t, :], top8[:, k, t, 0, :], ps[:, t, :], -GONE)
                    ins.then_inc(topk_scored, 1)
                    dve.wait_ge(topk_scored, ORDINAL[step])
                    for t in range(NT):
                        ins = nc.vector.max(top8[:, k, t, 1, :], left[:, k, t, :])
                    link(ins)
                    for t in range(NT):
                        ins = nc.vector.match_replace(left[:, k, t, :], top8[:, k, t, 1, :], left[:, k, t, :],
                                                      -GONE)
                    ins.then_inc(fin, 1)
                elif kind == "divide":
                    ps = misc.rearrange("p (s t g e) -> p s t g e", s=2, t=NT, g=4)
                    after(dve, "pe", step)
                    link(nc.vector.reciprocal(rden[:, b, :, :, :], ps[:, :, :, :, HD]))
                    for s in range(2):
                        ins = nc.vector.tensor_tensor(
                            z[:, b, :, :].rearrange("p t (g s e) -> p t g s e", g=4, s=4)[:, :, :, 2 * u + s, :],
                            ps[:, s, :, :, 0:HD],
                            rden[:, b, s, :, :].rearrange("p t (g o) -> p t g o", o=1).broadcast_to([P, NT, 4, HD]),
                            ALU.mult)
                    ins.then_inc(fin, 1)
                elif kind in ("residual", "down"):
                    lay = ATTN[l] if kind == "residual" else MLP[l]
                    bias = row_b[:, (PROJ_B if kind == "residual" else DOWN_B) + l:
                                 (PROJ_B if kind == "residual" else DOWN_B) + l + 1, :]
                    xb = x[:, b, :, :]
                    ps = misc[:, 0:NT * D].rearrange("p (t f) -> p t f", f=D)
                    after(dve, "pe", step)
                    if lay["gate"] is None:
                        link(nc.vector.tensor_tensor(z[:, b, :, :], ps, bias.broadcast_to([P, NT, D]), ALU.add))
                    else:
                        link(nc.vector.tensor_tensor(z[:, b, :, :], ps, bias.broadcast_to([P, NT, D]), ALU.add))
                        link(nc.vector.tensor_tensor(
                            z[:, b, :, :], z[:, b, :, :],
                            gate[:, b, lay["gate"]:lay["gate"] + 1, :].broadcast_to([P, NT, D]), ALU.mult))
                    nc.vector.tensor_tensor(xb, xb, z[:, b, :, :], ALU.add).then_inc(fin, 1)
                elif kind == "up_gate":
                    after(dve, "pe", step)
                    after(dve, "act", ("up", b, l, 0))
                    for j in range(4):
                        c = MLP[l]["bias"] + 4 + j
                        ins = nc.vector.scalar_tensor_tensor(
                            mixT[:, b, j, :], wide[:, SLOT[step], j, :], col_b[:, c:c + 1], mixT[:, b, j, :],
                            ALU.add, ALU.mult)
                    ins.then_inc(fin, 1)

        @block.tensor
        def _(pe):
            pe.wait_ge(s_in, 16 * (N_SMALL + 1))
            pe.wait_ge(s_init, 4)
            pe.wait_ge(s_cond, 4)
            pe.wait_ge(s_ctx, 16)
            for step in ORDER:
                kind, b, l, u = step
                fin = done.get((kind, "pe"))
                misc = misc2[:, SLOT[step], :] if PSUM_RING.get(kind) == "misc" else None
                if kind in PSUM_RING:
                    bank_free(pe, step)
                if kind == "mods":
                    blk = WAT[MODS[l][0]]
                    weights_in(pe, blk)
                    for n, j in enumerate(MODS[l][2] + MODS[l][3]):
                        ins = nc.tensor.matmul(misc[:, n * B:n * B + B], w[:, blk + j, :], cSilu[:],
                                               start=True, stop=True)
                    ins.then_inc(fin, 1)
                elif kind == "gates":
                    blk = WAT[MODS[l][0]]
                    for n, j in enumerate(MODS[l][4]):
                        ins = nc.tensor.matmul(misc[:, n * D:n * D + D], cWide[:, b, :], w[:, blk + j, :],
                                               start=True, stop=True)
                    ins.then_inc(fin, 1)
                elif kind in ("context", "normed"):
                    if kind == "normed":
                        after(pe, "dve", step)
                    src = z if kind == "normed" else ctx
                    for t in range(NT):
                        ins = nc.tensor.transpose(misc[:, P * t:P * t + P], src[:, b, t, :], ident[:])
                    ins.then_inc(fin, 1)
                elif kind in ("qk", "values"):
                    a = ATTN[l]
                    weights_in(pe, a["v"])
                    src = {"x": hT, "ctx_norm": hcT, "ctx": ctxT}[a["kv"]][:, b, :]
                    if a["kv"] == "ctx":
                        after(pe, "act", ("context", b, 0, 0))
                    elif a["kv"] == "ctx_norm":
                        after(pe, "act", ("normed", b, 10 + l, 0))
                    if kind == "qk":
                        after(pe, "act", ("normed", b, l, 0))
                        nc.tensor.matmul(misc[:, 0:N], w[:, a["q"], :], hT[:, b, :], start=True, stop=True)
                        ins = nc.tensor.matmul(misc[:, N:2 * N], w[:, a["k"], :], src, start=True, stop=True)
                    else:
                        for t in range(NT):
                            ins = nc.tensor.matmul(misc[:, D * t:D * t + D], src[:, P * t:P * t + P],
                                                   w[:, a["v"], :], start=True, stop=True)
                    ins.then_inc(fin, 1)
                elif kind in ("stack_q", "stack_k"):
                    c = 0 if kind == "stack_q" else 1
                    after(pe, "pool", ("qk", b, l, 0))
                    for s in range(4):
                        for half, part in enumerate((hi, lo)):
                            ins = nc.tensor.matmul(wide[:, SLOT[step], s, :], sel[:, c, half, s, :],
                                                   part[:, QK_SLOT[b, l, 0], c, :], start=(half == 0), stop=(half == 1))
                    ins.then_inc(fin, 1)
                elif kind in ("scores", "topk"):
                    s, g, h = head_of(u)
                    if u == 0:
                        after(pe, "dve", ("stack_k", b, l, 0))
                        after(pe, "act", ("stack_q", b, l, 0))
                        if ATTN[l]["kind"] == "window":
                            pe.wait_ge(window_q, WINDOW_NTH[b])
                    window = ATTN[l]["kind"] == "window"
                    for t in range(NT):
                        keys = slice(P * t, P * t + P) if window else slice(0, N)
                        ins = nc.tensor.matmul(score[:, SLOT[step], t, 0:P if window else N],
                                               QS[b][32 * g:32 * g + 32, s, P * t:P * t + P],
                                               KS[b][32 * g:32 * g + 32, s, keys], start=True, stop=True)
                    ins.then_inc(fin, 1)
                elif kind == "maxima":
                    after(pe, "dve", step)
                    nc.tensor.transpose(misc[:, 0:P],
                                        mhl[:, b, :, :, :, :].rearrange("p o g a c -> p (o g a c)").bitcast(F32),
                                        ident[:]).then_inc(fin, 1)
                elif kind == "weights":
                    if u == 0:
                        pe.wait_ge(max_rows_in[b], 16 * 4 * (l + 1))
                    s = u // 2
                    window = ATTN[l]["kind"] == "window"
                    for i in range(2):
                        g = 2 * (u % 2) + i
                        for t in range(NT):
                            queries = slice(P * t, P * t + P) if window else slice(0, N)
                            ins = nc.tensor.matmul(wide[:, SLOT[step], 2 * i + t, 0:P if window else N],
                                                   KS[b][32 * g:32 * g + 32, s, P * t:P * t + P],
                                                   QS[b][32 * g:32 * g + 32, s, queries], start=True, stop=True)
                    ins.then_inc(fin, 1)
                elif kind == "turned":
                    for i in range(2):
                        head = ("topk", b, l, 2 * u + i)
                        after(pe, "pool", head)
                        for t in range(NT):
                            for r in range(NT):
                                ins = nc.tensor.transpose(wide[:, SLOT[step], 2 * i + t, P * r:P * r + P],
                                                          picked[:, SEL_SLOT[head], r, P * t:P * t + P], ident[:])
                    ins.then_inc(fin, 1)
                elif kind == "mix":
                    filled = "turned" if ATTN[l]["kind"] == "topk" else "weights"
                    after(pe, "act", (filled, b, l, 2 * u + 1))
                    if u == 0:
                        after(pe, "dve", ("values", b, l, 0))
                    for i in range(4):
                        s, g, h = head_of(4 * u + i)
                        window = ATTN[l]["kind"] == "window"
                        for t in range(NT):
                            queries = slice(P * t, P * t + P) if window else slice(0, N)
                            ins = nc.tensor.matmul(misc[32 * g:32 * g + 32, queries],
                                                   V[:, b, t, 9 * h:9 * h + 32],
                                                   pT[:, PT_SLOT[b, l, 2 * u + i // 2], 2 * (i % 2) + t,
                                                      0:P if window else N],
                                                   start=(t == 0 or window), stop=(t == NT - 1 or window),
                                                   tile_position=(0, 32 * g))
                    ins.then_inc(fin, 1)
                elif kind == "divide":
                    after(pe, "act", ("mix", b, l, 2 * u + 1))
                    for s in range(2):
                        for t in range(NT):
                            n = (NT * s + t) * P
                            ins = nc.tensor.transpose(misc[:, n:n + P], mixT[:, b, 2 * u + s, P * t:P * t + P],
                                                      ident[:])
                    ins.then_inc(fin, 1)
                elif kind == "heads_out":
                    after(pe, "dve", ("divide", b, l, 1))
                    for t in range(NT):
                        ins = nc.tensor.transpose(misc[:, P * t:P * t + P], z[:, b, t, :], ident[:])
                    ins.then_inc(fin, 1)
                elif kind == "residual":
                    weights_in(pe, ATTN[l]["o"])
                    after(pe, "act", ("heads_out", b, l, 0))
                    for t in range(NT):
                        ins = nc.tensor.matmul(misc[:, D * t:D * t + D], hT[:, b, P * t:P * t + P],
                                               w[:, ATTN[l]["o"], :], start=True, stop=True)
                    ins.then_inc(fin, 1)
                elif kind in ("up", "up_gate"):
                    blk = MLP[l]["up"] + (4 if kind == "up_gate" else 0)
                    after(pe, "act", ("normed", b, 7 + l, 0))
                    for j in range(4):
                        ins = nc.tensor.matmul(wide[:, SLOT[step], j, :], w[:, blk + j, :], hT[:, b, :],
                                               start=True, stop=True)
                    ins.then_inc(fin, 1)
                elif kind == "down":
                    if MLP[l]["act"] == "swiglu":
                        after(pe, "dve", ("up_gate", b, l, 0))
                    else:
                        after(pe, "act", ("up", b, l, 0))
                    for t in range(NT):
                        for j in range(4):
                            ins = nc.tensor.matmul(misc[:, D * t:D * t + D], mixT[:, b, j, P * t:P * t + P],
                                                   w[:, MLP[l]["down"] + j, :], start=(j == 0), stop=(j == 3))
                    ins.then_inc(fin, 1)


def kernel(**inputs):
    import numpy as _np
    import concourse.bacc as _bacc
    from concourse import mybir as _mybir
    from concourse.bass_utils import run_bass_kernel_spmd as _run

    nc = _bacc.Bacc("TRN2", target_bir_lowering=False, num_devices=1)
    a = {k: _np.asarray(v) for k, v in inputs.items()}
    blocks = []
    for name, k in WEIGHTS:
        m = a[name]
        if m.shape[0] == D:
            blocks.append(m.reshape(D, k, D))
        else:
            blocks.append(m.reshape(k, D, D).transpose(1, 0, 2))
    arrays = {
        "x": a["x"], "cond": _np.ascontiguousarray(a["cond_1024"].T), "ctx": a["ctx_1024"],
        "w": _np.ascontiguousarray(_np.concatenate(blocks, axis=1)),
        "rows": _np.ascontiguousarray(_np.concatenate([a[n][D * j:D * (j + k)] for n, j, k in ROW_BIASES])),
        "cols": _np.ascontiguousarray(
            _np.concatenate([a[n][D * j:D * (j + k)].reshape(k, D) for n, j, k in COL_BIASES]).T),
    }
    arrays.update(constants())
    args = []
    for name, v in arrays.items():
        args.append(nc.dram_tensor(f"in_{name}", v.shape, _mybir.dt.from_np(v.dtype), kind="ExternalInput").ap())
    out = nc.dram_tensor("out_0", (B, N, D), F32, kind="ExternalOutput").ap()
    build(nc, *args, out)
    r = _run(nc, [{f"in_{k}": v for k, v in arrays.items()}], core_ids=[0])
    return r.results[0]["out_0"]
```
